# Optimizing a Trainium2 kernel written in Bass

```python
import numpy as np
import jax
import jax.numpy as jnp

def _softmax(x, axis=-1):
    return jax.nn.softmax(x, axis=axis)
def _gelu(x):
    return jax.nn.gelu(x, approximate=True)
def _silu(x):
    return jax.nn.silu(x)
def _sigmoid(x):
    return jax.nn.sigmoid(x)
def _layernorm(x, axis=-1, eps=1e-5):
    m = jnp.mean(x, axis=axis, keepdims=True)
    v = jnp.var(x, axis=axis, keepdims=True)
    return (x - m) / jnp.sqrt(v + eps)
def _scatter_add(tgt, idx, src, axis=0):
    return tgt.at[idx].add(src)
def _segment_sum(src, seg, n):
    return jax.ops.segment_sum(src, seg, n)

kernel_name = 'mk_conv_seq_d1_conv_nhwc256_f4589f'

def setup_inputs(seed: int = 0):
    np.random.seed(seed)
    _w = jnp.asarray
    def _rec_inputs():
        import jax
        import jax.numpy as jnp
        _gk = jax.random.key(seed)
        x = -0.0003929 + 0.9999 * jax.random.normal(jax.random.fold_in(_gk, 1), (4, 64, 256, 256), jnp.float32)
        return x
    x = _rec_inputs()
    def _L0_conv_setup():
        import jax, jax.numpy as jnp
        import numpy as np
        import math
        B, D_MODEL, EMB, ORDER, SEQ = (4, 64, 33, 64, 256)
        TARGET, FAST_PCT, SLOW_PCT = (0.01, 0.3, 1.5)

        def _pos_emb(L, emb_dim):
            t = jnp.linspace(0.0, 1.0, L)[None, :, None]
            bands = (emb_dim - 1) // 2
            t_r = jnp.linspace(0.0, L - 1.0, L)[None, :, None]
            w = 2.0 * math.pi * t_r / L
            f = jnp.linspace(0.0001, bands - 1.0, bands)[None, None]
            zc = jnp.exp(-1j * f * w)
            z = jnp.concatenate([t, zc.real, zc.imag], axis=-1)
            return (z.astype(jnp.float32), t.astype(jnp.float32))

        def _implicit_filter(z, w1, b1, w2, b2, w3, b3, wo, freq, t, deltas):
            h = jnp.sin(freq * (z @ w1 + b1))
            h = jnp.sin(freq * (h @ w2 + b2))
            h = jnp.sin(freq * (h @ w3 + b3))
            h = h @ wo
            decay = jnp.exp(-t * jnp.abs(deltas))
            return h * decay
        key = jax.random.key(seed)
        ks = jax.random.split(key, 24)
        z, _ = _pos_emb(SEQ, EMB)

        def lin(k, fan_in, fan_out):
            return jax.random.normal(k, (fan_in, fan_out), jnp.float32) / np.sqrt(fan_in)
        inp = {'x': jax.random.normal(ks[0], (B, D_MODEL, SEQ, SEQ), jnp.float32), 'z': z, 'Xw1': lin(ks[1], EMB, ORDER), 'Xb1': jax.random.normal(ks[2], (ORDER,), jnp.float32) * 0.02, 'Xw2': lin(ks[3], ORDER, ORDER), 'Xb2': jax.random.normal(ks[4], (ORDER,), jnp.float32) * 0.02, 'Xw3': lin(ks[5], ORDER, ORDER), 'Xb3': jax.random.normal(ks[6], (ORDER,), jnp.float32) * 0.02, 'Xwo': lin(ks[7], ORDER, D_MODEL), 'Xfreq': jnp.ones((1, ORDER), jnp.float32), 'Yw1': lin(ks[8], EMB, ORDER), 'Yb1': jax.random.normal(ks[9], (ORDER,), jnp.float32) * 0.02, 'Yw2': lin(ks[10], ORDER, ORDER), 'Yb2': jax.random.normal(ks[11], (ORDER,), jnp.float32) * 0.02, 'Yw3': lin(ks[12], ORDER, ORDER), 'Yb3': jax.random.normal(ks[13], (ORDER,), jnp.float32) * 0.02, 'Ywo': lin(ks[14], ORDER, D_MODEL), 'Yfreq': jnp.ones((1, ORDER), jnp.float32), 'bias': jax.random.normal(ks[15], (D_MODEL,), jnp.float32), 'L': SEQ}
        return inp
    _L0_conv_all = _L0_conv_setup()
    _L0_conv_in = {k: v for k, v in _L0_conv_all.items() if k in ('z', 'Xw1', 'Xb1', 'Xw2', 'Xb2', 'Xw3', 'Xb3', 'Xwo', 'Xfreq', 'Yw1', 'Yb1', 'Yw2', 'Yb2', 'Yw3', 'Yb3', 'Ywo', 'Yfreq', 'bias', )}
    del _L0_conv_all

    return {
        "x": x,
        "L0_conv_z": _L0_conv_in["z"],
        "L0_conv_Xw1": _L0_conv_in["Xw1"],
        "L0_conv_Xb1": _L0_conv_in["Xb1"],
        "L0_conv_Xw2": _L0_conv_in["Xw2"],
        "L0_conv_Xb2": _L0_conv_in["Xb2"],
        "L0_conv_Xw3": _L0_conv_in["Xw3"],
        "L0_conv_Xb3": _L0_conv_in["Xb3"],
        "L0_conv_Xwo": _L0_conv_in["Xwo"],
        "L0_conv_Xfreq": _L0_conv_in["Xfreq"],
        "L0_conv_Yw1": _L0_conv_in["Yw1"],
        "L0_conv_Yb1": _L0_conv_in["Yb1"],
        "L0_conv_Yw2": _L0_conv_in["Yw2"],
        "L0_conv_Yb2": _L0_conv_in["Yb2"],
        "L0_conv_Yw3": _L0_conv_in["Yw3"],
        "L0_conv_Yb3": _L0_conv_in["Yb3"],
        "L0_conv_Ywo": _L0_conv_in["Ywo"],
        "L0_conv_Yfreq": _L0_conv_in["Yfreq"],
        "L0_conv_bias": _L0_conv_in["bias"],
    }

def reference(x, L0_conv_z, L0_conv_Xw1, L0_conv_Xb1, L0_conv_Xw2, L0_conv_Xb2, L0_conv_Xw3, L0_conv_Xb3, L0_conv_Xwo, L0_conv_Xfreq, L0_conv_Yw1, L0_conv_Yb1, L0_conv_Yw2, L0_conv_Yb2, L0_conv_Yw3, L0_conv_Yb3, L0_conv_Ywo, L0_conv_Yfreq, L0_conv_bias):
    import jax
    import jax.numpy as jnp
    def _L0_conv_ref(x, z, Xw1, Xb1, Xw2, Xb2, Xw3, Xb3, Xwo, Xfreq, Yw1, Yb1, Yw2, Yb2, Yw3, Yb3, Ywo, Yfreq, bias, L):
        import jax, jax.numpy as jnp
        import numpy as np
        import math
        B, D_MODEL, EMB, ORDER, SEQ = (4, 64, 33, 64, 256)
        TARGET, FAST_PCT, SLOW_PCT = (0.01, 0.3, 1.5)

        def _pos_emb(L, emb_dim):
            t = jnp.linspace(0.0, 1.0, L)[None, :, None]
            bands = (emb_dim - 1) // 2
            t_r = jnp.linspace(0.0, L - 1.0, L)[None, :, None]
            w = 2.0 * math.pi * t_r / L
            f = jnp.linspace(0.0001, bands - 1.0, bands)[None, None]
            zc = jnp.exp(-1j * f * w)
            z = jnp.concatenate([t, zc.real, zc.imag], axis=-1)
            return (z.astype(jnp.float32), t.astype(jnp.float32))

        def _implicit_filter(z, w1, b1, w2, b2, w3, b3, wo, freq, t, deltas):
            h = jnp.sin(freq * (z @ w1 + b1))
            h = jnp.sin(freq * (h @ w2 + b2))
            h = jnp.sin(freq * (h @ w3 + b3))
            h = h @ wo
            decay = jnp.exp(-t * jnp.abs(deltas))
            return h * decay
        d_model = x.shape[1]
        t = jnp.linspace(0.0, 1.0, L)[None, :, None].astype(jnp.float32)
        max_dec = math.log(TARGET) / FAST_PCT
        min_dec = math.log(TARGET) / SLOW_PCT
        deltas = jnp.linspace(min_dec, max_dec, d_model)[None, None].astype(jnp.float32)
        hx = _implicit_filter(z, Xw1, Xb1, Xw2, Xb2, Xw3, Xb3, Xwo, Xfreq, t, deltas)
        hy = _implicit_filter(z, Yw1, Yb1, Yw2, Yb2, Yw3, Yb3, Ywo, Yfreq, t, deltas)
        k = jnp.einsum('ijk,imk->ijmk', hx, hy)[0]
        k = jnp.transpose(k, (2, 0, 1))
        fft_size = 2 * L
        k_f = jnp.fft.rfft2(k, s=(fft_size, fft_size)) / fft_size
        u_f = jnp.fft.rfft2(x.astype(jnp.float32), s=(fft_size, fft_size))
        y = jnp.fft.irfft2(u_f * k_f, s=(fft_size, fft_size))[..., :L, :L]
        out = y + x * bias[:, None, None]
        return out.astype(x.dtype)

    def _gn(v, G=32, eps=1e-5):
        B_, H_, W_, C_ = v.shape
        g = v.reshape(B_, H_, W_, G, C_ // G)
        m = jnp.mean(g, axis=(1, 2, 4), keepdims=True)
        s = jnp.var(g, axis=(1, 2, 4), keepdims=True)
        return ((g - m) / jnp.sqrt(s + eps)).reshape(v.shape)

    def _ln_c(v, eps=1e-6):
        m = jnp.mean(v, axis=-1, keepdims=True)
        s = jnp.var(v, axis=-1, keepdims=True)
        return (v - m) / jnp.sqrt(s + eps)

    def _ln_t(v, eps=1e-5):
        m = jnp.mean(v, axis=-1, keepdims=True)
        s = jnp.var(v, axis=-1, keepdims=True)
        return (v - m) / jnp.sqrt(s + eps)

    def _to_tokens(v):
        B_, H_, W_, C_ = v.shape
        return v.reshape(B_, H_ * W_, C_)
    def _from_tokens(t, like):
        return t.reshape(like.shape)

    x = _L0_conv_ref(x, L0_conv_z, L0_conv_Xw1, L0_conv_Xb1, L0_conv_Xw2, L0_conv_Xb2, L0_conv_Xw3, L0_conv_Xb3, L0_conv_Xwo, L0_conv_Xfreq, L0_conv_Yw1, L0_conv_Yb1, L0_conv_Yw2, L0_conv_Yb2, L0_conv_Yw3, L0_conv_Yb3, L0_conv_Ywo, L0_conv_Yfreq, L0_conv_bias, 256)
    return x


_drawn_inputs = setup_inputs


def setup_inputs(seed=0):
    import zlib

    import numpy as np

    out = dict(_drawn_inputs(seed))
    spreads = {'L0_conv_Xfreq': (1.0, 0.6), 'L0_conv_Yfreq': (1.0, 0.6)}
    factors = {'L0_conv_z': 7.879,
     'L0_conv_Xw1': 7.804,
     'L0_conv_Xb1': 8.0,
     'L0_conv_Xw2': 7.846,
     'L0_conv_Xb2': 8.0,
     'L0_conv_Xw3': 7.545,
     'L0_conv_Xb3': 8.0,
     'L0_conv_Xwo': 7.489,
     'L0_conv_Yw1': 7.49,
     'L0_conv_Yb1': 8.0,
     'L0_conv_Yw2': 6.866,
     'L0_conv_Yb2': 8.0,
     'L0_conv_Yw3': 7.297,
     'L0_conv_Yb3': 8.0,
     'L0_conv_Ywo': 7.44}
    for name, (base, spread) in spreads.items():
        noise = np.random.default_rng([zlib.crc32(name.encode()), seed]).standard_normal(out[name].shape)
        drawn = base * np.exp(spread * noise) if base else spread * noise
        out[name] = jnp.asarray(drawn.astype(out[name].dtype))
    for name, factor in factors.items():
        out[name] = (out[name] * factor).astype(out[name].dtype)
    return out
```

```python
import math
from contextlib import ExitStack

import numpy as np

import concourse.bass as bass
from concourse import mybir

F32 = mybir.dt.float32
F32R = mybir.dt.float32r
ALU = mybir.AluOpType
ACT = mybir.ActivationFunctionType

P = 128
H = P
TWO_PI = 2.0 * math.pi
PI_A = 6.28125
PI_B = 0.0019350051879882812
PI_C = TWO_PI - PI_A - PI_B
ROUND = 1.5 * 2.0 ** 23
PI_INSIDE = 3.1415925

LAYERS = 3
RING = 4
BODY = 8
LEAD = 2


def decay_table(seq, channels, fft_size):
    t = np.linspace(0.0, 1.0, seq).astype(np.float32)
    deltas = np.linspace(math.log(0.01) / 1.5, math.log(0.01) / 0.3, channels).astype(np.float32)
    decay = np.exp(-(t[None, :] * np.abs(deltas)[:, None])).astype(np.float32)
    return np.concatenate([decay, decay / np.float32(fft_size)], axis=0)


def backwards(ap):
    step, count = ap.ap[-1]
    return bass.AP(ap.tensor, ap.offset + step * (count - 1), [*ap.ap[:-1], [-step, count]])


def build_program(nc, x, z_t, first_w, mid_w, out_w, columns, bias, decay, out):
    B, C, S, _ = x.shape
    E = z_t.shape[0]
    N = B * C
    ORDER = mid_w[0][0].shape[0]
    assert S == 2 * H and 2 * C == P and 2 * ORDER == P and B == RING and BODY == 2 * B
    ITERS = N // BODY
    PAIRS = BODY // 2
    GROW = S + P

    grev = nc.dram_tensor("filters_reversed", (P, GROW), F32, kind="Internal").ap()

    with ExitStack() as ctx:
        def sb(name, shape, dt=F32):
            return ctx.enter_context(nc.sbuf_tensor(name, shape, dt))

        def sem(name):
            return ctx.enter_context(nc.semaphore(name))

        zt = sb("zt", [P, S])
        w_first = sb("w_first", [P, ORDER])
        w_mid = sb("w_mid", [P, LAYERS - 1, ORDER])
        w_out = sb("w_out", [P, C])
        cols = sb("cols", [P, LAYERS + 1])
        decay_sb = sb("decay_sb", [P, S])
        bias_bc = sb("bias_bc", [P, C])
        angle = sb("angle", [P, S])
        turns = sb("turns", [P, S])
        whole = sb("whole", [P, S])
        red = sb("red", [P, 3, S])
        hidden = sb("hidden", [P, S])
        grow = sb("grow", [P, GROW])

        x_raw = sb("x_raw", [P, BODY, 2, S])
        x_hi = sb("x_hi", [P, RING, S], F32R)
        x_lo = sb("x_lo", [P, RING, S], F32R)
        z_hi = sb("z_hi", [P, RING, S], F32R)
        z_lo = sb("z_lo", [P, RING, S], F32R)
        z_raw = sb("z_raw", [P, RING, S])
        y_out = sb("y_out", [P, BODY, 2, S])
        t_stage = sb("t_stage", [P, 2, 2, S])
        t_hi = sb("t_hi", [P, 2, 2, S], F32R)
        t_lo = sb("t_lo", [P, 2, 2, S], F32R)
        t_raw = sb("t_raw", [P, 2, 2, H])

        psz = ctx.enter_context(nc.psum_tensor("psz", [P, RING, 2, S], F32))
        psy = ctx.enter_context(nc.psum_tensor("psy", [P, RING, 2, S], F32))

        params_landed = sem("params_landed")
        mlp_product = sem("mlp_product")
        mlp_step = sem("mlp_step")
        mlp_reduced = sem("mlp_reduced")
        mlp_sine = sem("mlp_sine")
        rows_ready = sem("rows_ready")
        rows_stored = sem("rows_stored")
        x_landed = [sem(f"x_landed{q}") for q in range(PAIRS)]
        t_landed = [sem(f"t_landed{q}") for q in range(2)]
        y_stored = [sem(f"y_stored{q}") for q in range(PAIRS)]
        t_hi_done = sem("t_hi_done")
        t_split = sem("t_split")
        x_hi_done = sem("x_hi_done")
        x_split = sem("x_split")
        z_product = sem("z_product")
        z_hi_done = sem("z_hi_done")
        z_lo_done = sem("z_lo_done")
        y_product = sem("y_product")
        y_done = sem("y_done")

        halves = [slice(0, ORDER), slice(ORDER, P)]
        param_loads = [(bias_bc[:, :], bias.partition_broadcast(P)), (decay_sb[:, :], decay)]
        for f, rows in enumerate(halves):
            param_loads.append((zt[rows.start:rows.start + E, :], z_t))
            param_loads.append((w_first[rows.start:rows.start + E, :], first_w[f]))
            param_loads += [(w_mid[rows, l, :], mid_w[f][l]) for l in range(LAYERS - 1)]
            param_loads.append((w_out[rows, :], out_w[f]))
            param_loads += [(cols[rows, l:l + 1], columns[f][l]) for l in range(LAYERS + 1)]

        block = ctx.enter_context(nc.Block())

        @block.sync
        def _(sp):
            def load_x(channel, slot):
                for s in (slot, slot + 1):
                    src = x[s % B, bass.ds(channel, 1), :, :].rearrange("o (k p) j -> p (o k) j", p=P)
                    sp.dma_start(x_raw[:, s, :, :], src).then_inc(x_landed[slot // 2], 16)

            def store_y(channel, slot):
                for s in (slot, slot + 1):
                    dst = out[s % B, bass.ds(channel, 1), :, :].rearrange("o (k p) j -> p (o k) j", p=P)
                    sp.dma_start(dst, y_out[:, s, :, :]).then_inc(y_stored[slot // 2], 16)

            def load_t(channel, parity):
                src = bass.AP(grev.tensor, channel * GROW, [[1, P], [C * GROW, 2], [1, S]])
                sp.dma_start(t_stage[:, parity, :, :], src).then_inc(t_landed[parity], 16)

            for dst, src in param_loads:
                sp.dma_start(dst, src).then_inc(params_landed, 16)
            for slot in range(0, BODY, 2):
                load_x(slot // B, slot)
            sp.wait_ge(rows_ready, 2)
            sp.dma_start(grev, grow[:, :]).then_inc(rows_stored, 16)
            sp.wait_ge(rows_stored, 16)
            load_t(0, 0)
            load_t(1, 1)

            def iteration(i, last):
                if not last:
                    sp.wait_ge(t_split, 2 * i + 1)
                    load_t(2 * i + 2, 0)
                for m in range(1, BODY, 2):
                    sp.wait_ge(y_done, BODY * i + m + 1)
                    store_y(2 * i + m // B, m - 1)
                    if not last:
                        load_x(2 * i + 2 + m // B, m - 1)
                    if m == 1 and not last:
                        sp.wait_ge(t_split, 2 * i + 2)
                        load_t(2 * i + 3, 1)

            with sp.Fori(0, ITERS - 1) as i:
                iteration(i, False)
            iteration(ITERS - 1, True)
            for q in range(PAIRS):
                sp.wait_ge(y_stored[q], 32 * (ITERS + 1))

        @block.tensor
        def _(pe):
            pe.wait_ge(params_landed, 16 * len(param_loads))
            for l in range(LAYERS + 1):
                if l:
                    pe.wait_ge(mlp_sine, l)
                for rows in halves:
                    k = slice(rows.start, rows.start + E) if l == 0 else rows
                    w = w_first[k, :] if l == 0 else w_mid[k, l - 1, :] if l < LAYERS else w_out[k, :]
                    src = zt[k, :] if l == 0 else hidden[k, :]
                    mm = pe.matmul(psz[rows, l, 0, :], w, src, start=True, stop=True)
                mm.then_inc(mlp_product, 1)

            def product(ps, hi, lo, raw, parity, f):
                pe.matmul(ps, hi, t_hi[:, parity, f, :], start=True, stop=False)
                pe.matmul(ps, hi, t_lo[:, parity, f, :], start=False, stop=False)
                pe.matmul(ps, lo, t_hi[:, parity, f, :], start=False, stop=False)
                return pe.matmul(ps[:, 0:H], raw, t_raw[:, parity, f, :], start=False, stop=True)

            def stage1(i, m):
                s, parity = m % BODY, m // B % 2
                if m % 2 == 0:
                    pe.wait_ge(x_split, PAIRS * i + m // 2 + 1)
                if m % B == 0:
                    pe.wait_ge(t_split, 2 * i + m // B + 1)
                for jc in range(2):
                    j = slice(jc * P, jc * P + P)
                    mm = product(psz[:, s % RING, jc, :], x_hi[:, s % RING, j], x_lo[:, s % RING, j],
                                 x_raw[:, s, 1, j], parity, 0)
                mm.then_inc(z_product, 1)

            def stage2(i, m):
                s, parity = m % RING, m // B % 2
                pe.wait_ge(z_lo_done, BODY * i + m + 1)
                for ic in range(2):
                    r = slice(ic * P, ic * P + P)
                    mm = product(psy[:, s, ic, :], z_hi[:, s, r], z_lo[:, s, r], z_raw[:, s, r], parity, 1)
                mm.then_inc(y_product, 1)

            for m in range(LEAD):
                stage1(0, m)

            def iteration(i, last):
                for m in range(BODY):
                    if not last or m + LEAD < BODY:
                        stage1(i, m + LEAD)
                    stage2(i, m)

            with pe.Fori(0, ITERS - 1) as i:
                iteration(i, False)
            iteration(ITERS - 1, True)

        @block.scalar
        def _(act):
            for l in range(LAYERS):
                act.wait_ge(mlp_reduced, l + 1)
                nc.scalar.activation(hidden[:, :], red[:, 2, :], ACT.Sin).then_inc(mlp_sine, 1)

            def split_t(channel, parity, landed):
                act.wait_ge(t_landed[parity], landed)
                nc.scalar.copy(t_raw[:, parity, :, :], t_stage[:, parity, :, H:S])
                nc.scalar.copy(t_hi[:, parity, :, :], t_stage[:, parity, :, :]).then_inc(t_hi_done, 1)

            def split_x(slot, landed):
                act.wait_ge(x_landed[slot // 2], landed)
                r = slot % RING
                nc.scalar.copy(x_hi[:, r:r + 2, :], x_raw[:, slot:slot + 2, 0, :]).then_inc(x_hi_done, 1)

            def evacuate(i, m):
                s = m % RING
                act.wait_ge(z_product, BODY * i + m + 1)
                nc.scalar.copy(z_raw[:, s, :], backwards(psz[:, s, 1, :]))
                nc.scalar.copy(z_hi[:, s, :], backwards(psz[:, s, 0, :])).then_inc(z_hi_done, 1)

            split_x(0, 32)
            split_x(2, 32)
            split_t(0, 0, 16)
            for m in range(LEAD):
                evacuate(0, m)

            def iteration(i, last):
                for m in range(BODY):
                    if not last or m + LEAD < BODY:
                        evacuate(i, m + LEAD)
                    if m % 2 == 0 and not (last and m + RING >= BODY):
                        split_x((m + RING) % BODY, 32 * (i + 1 + (m + RING) // BODY))
                    if m == 0:
                        split_t(2 * i + 1, 1, 16 * (i + 1))
                    if m == B and not last:
                        split_t(2 * i + 2, 0, 16 * (i + 2))

            with act.Fori(0, ITERS - 1) as i:
                iteration(i, False)
            iteration(ITERS - 1, True)

        @block.vector
        def _(dve):
            steps = [0]

            def step(ins):
                steps[0] += 1
                ins.then_inc(mlp_step, 1)
                dve.wait_ge(mlp_step, steps[0])

            for q in range(PAIRS):
                dve.sem_inc(y_stored[q], 32)
            nc.vector.memset(grow[:, S:GROW], 0.0).then_inc(rows_ready, 1)
            dve.wait_ge(params_landed, 16 * len(param_loads))
            for l in range(LAYERS):
                dve.wait_ge(mlp_product, l + 1)
                step(nc.vector.tensor_scalar(angle[:, :], psz[:, l, 0, :], cols[:, l:l + 1],
                                             cols[:, LAYERS:LAYERS + 1], ALU.add, ALU.mult))
                step(nc.vector.tensor_scalar(turns[:, :], angle[:, :], 1.0 / TWO_PI, ROUND, ALU.mult, ALU.add))
                step(nc.vector.tensor_scalar(whole[:, :], turns[:, :], ROUND, None, ALU.subtract))
                step(nc.vector.scalar_tensor_tensor(out=red[:, 0, :], in0=whole[:, :], scalar=-PI_A,
                                                    in1=angle[:, :], op0=ALU.mult, op1=ALU.add))
                step(nc.vector.scalar_tensor_tensor(out=red[:, 1, :], in0=whole[:, :], scalar=-PI_B,
                                                    in1=red[:, 0, :], op0=ALU.mult, op1=ALU.add))
                step(nc.vector.scalar_tensor_tensor(out=red[:, 0, :], in0=whole[:, :], scalar=-PI_C,
                                                    in1=red[:, 1, :], op0=ALU.mult, op1=ALU.add))
                nc.vector.tensor_scalar(red[:, 2, :], red[:, 0, :], PI_INSIDE, -PI_INSIDE,
                                        ALU.min, ALU.max).then_inc(mlp_reduced, 1)
            dve.wait_ge(mlp_product, LAYERS + 1)
            nc.vector.tensor_tensor(backwards(grow[:, 0:S]), psz[:, LAYERS, 0, :], decay_sb[:, :],
                                    ALU.mult).then_inc(rows_ready, 1)

            def split_t(channel, parity):
                dve.wait_ge(t_hi_done, channel + 1)
                nc.vector.tensor_tensor(t_lo[:, parity, :, :], t_stage[:, parity, :, :],
                                        t_hi[:, parity, :, :].bitcast(F32), ALU.subtract).then_inc(t_split, 1)

            def split_x(pair, slot):
                dve.wait_ge(x_hi_done, pair + 1)
                r = slot % RING
                nc.vector.tensor_tensor(x_lo[:, r:r + 2, :], x_raw[:, slot:slot + 2, 0, :],
                                        x_hi[:, r:r + 2, :].bitcast(F32), ALU.subtract).then_inc(x_split, 1)

            def split_z(i, m):
                s = m % RING
                dve.wait_ge(z_hi_done, BODY * i + m + 1)
                nc.vector.tensor_tensor(z_lo[:, s, :], backwards(psz[:, s, 0, :]), z_hi[:, s, :].bitcast(F32),
                                        ALU.subtract).then_inc(z_lo_done, 1)

            def finish_y(i, m):
                dve.wait_ge(y_product, BODY * i + m + 1)
                if m % 2 == 0:
                    dve.wait_ge(y_stored[m // 2], 32 * (i + 1))
                nc.vector.scalar_tensor_tensor(out=y_out[:, m, :, :], in0=x_raw[:, m, :, :],
                                               scalar=bias_bc[:, bass.ds(2 * i + m // B, 1)],
                                               in1=backwards(psy[:, m % RING, :, :]),
                                               op0=ALU.mult, op1=ALU.add).then_inc(y_done, 1)

            split_x(0, 0)
            split_x(1, 2)
            split_t(0, 0)
            for m in range(LEAD):
                split_z(0, m)

            def iteration(i, last):
                for m in range(BODY):
                    if not last or m + LEAD < BODY:
                        split_z(i, m + LEAD)
                    if m % 2 == 0 and not (last and m + RING >= BODY):
                        split_x(PAIRS * i + (m + RING) // 2, (m + RING) % BODY)
                    if m == 0:
                        split_t(2 * i + 1, 1)
                    if m == B and not last:
                        split_t(2 * i + 2, 0)
                    finish_y(i, m)

            with dve.Fori(0, ITERS - 1) as i:
                iteration(i, False)
            iteration(ITERS - 1, True)


def kernel(**inputs):
    import concourse.bacc as _bacc
    from concourse.bass_utils import run_bass_kernel_spmd as _run

    nc = _bacc.Bacc("TRN2", target_bir_lowering=False, num_devices=1)
    arrays = {}

    def given(name, a):
        a = np.ascontiguousarray(a)
        arrays[name] = a
        return nc.dram_tensor(name, a.shape, mybir.dt.from_np(a.dtype), kind="ExternalInput").ap()

    x = np.asarray(inputs["x"])
    _, channels, seq, _ = x.shape

    def weight(f, name):
        return given(f"{f}{name}", inputs[f"L0_conv_{f}{name}"])

    def column(f, name):
        return given(f"{f}{name}", np.asarray(inputs[f"L0_conv_{f}{name}"]).reshape(-1, 1))

    args = [
        given("x_dram", x),
        given("z_t", np.asarray(inputs["L0_conv_z"])[0].T),
        [weight(f, "w1") for f in "XY"],
        [[weight(f, "w2"), weight(f, "w3")] for f in "XY"],
        [weight(f, "wo") for f in "XY"],
        [[column(f, n) for n in ("b1", "b2", "b3", "freq")] for f in "XY"],
        given("bias_dram", inputs["L0_conv_bias"]),
        given("decay", decay_table(seq, channels, 2 * seq)),
    ]
    out = nc.dram_tensor("out_dram", x.shape, mybir.dt.from_np(x.dtype), kind="ExternalOutput").ap()
    build_program(nc, *args, out)
    r = _run(nc, [arrays], core_ids=[0])
    return r.results[0]["out_dram"]
```

```python
import math
from contextlib import ExitStack

import numpy as np

import concourse.bass as bass
from concourse import mybir

F32 = mybir.dt.float32
F32R = mybir.dt.float32r
ALU = mybir.AluOpType
ACT = mybir.ActivationFunctionType

P = 128
H = P
TWO_PI = 2.0 * math.pi
PI_A = 6.28125
PI_B = TWO_PI - PI_A
ROUND = 1.5 * 2.0 ** 23
PI_INSIDE = 3.1415925

LAYERS = 3
RING = 4
BODY = 16
LEAD = 2
WARM_START, WARM_LAYER, WARM_WAIT = 4, 11, 28


def decay_table(seq, channels, fft_size):
    t = np.linspace(0.0, 1.0, seq).astype(np.float32)
    deltas = np.linspace(math.log(0.01) / 1.5, math.log(0.01) / 0.3, channels).astype(np.float32)
    decay = np.exp(-(t[None, :] * np.abs(deltas)[:, None])).astype(np.float32)
    return np.concatenate([decay, decay / np.float32(fft_size)], axis=0)


def backwards(ap):
    step, count = ap.ap[-1]
    return bass.AP(ap.tensor, ap.offset + step * (count - 1), [*ap.ap[:-1], [-step, count]])


def build_program(nc, x, networks, bias, decay, out, E, ORDER):
    B, C, S, _ = x.shape
    N = B * C
    assert S == 2 * H and 2 * C == P and 2 * ORDER == P and B == RING and BODY % (2 * B) == 0 and BODY > 2 * B
    ITERS = N // BODY
    CHANNELS = BODY // B
    PAIRS = BODY // 2
    GROW = S + P

    grev = nc.dram_tensor("filters_reversed", (P, GROW), F32, kind="Internal").ap()

    with ExitStack() as ctx:
        def sb(name, shape, dt=F32):
            return ctx.enter_context(nc.sbuf_tensor(name, shape, dt))

        def sem(name):
            return ctx.enter_context(nc.semaphore(name))

        nets = sb("nets", [P, networks.shape[1]])
        zt = nets[:, 0:S]
        weights = [nets[:, S + l * ORDER:S + (l + 1) * ORDER] for l in range(LAYERS + 1)]
        cols = nets[:, S + (LAYERS + 1) * ORDER:]
        decay_sb = sb("decay_sb", [P, S])
        bias_bc = sb("bias_bc", [P, C])
        angle = sb("angle", [P, S])
        turns = sb("turns", [P, S])
        whole = sb("whole", [P, S])
        red = sb("red", [P, 3, S])
        hidden = sb("hidden", [P, S])
        grow = sb("grow", [P, GROW])
        idle = sb("idle", [P, 2 * S], mybir.dt.bfloat16)

        x_raw = sb("x_raw", [P, BODY, 2, S])
        x_hi = sb("x_hi", [P, RING, S], F32R)
        x_lo = sb("x_lo", [P, RING, S], F32R)
        z_hi = sb("z_hi", [P, RING, S], F32R)
        z_lo = sb("z_lo", [P, RING, S], F32R)
        z_raw = sb("z_raw", [P, RING, S])
        y_out = sb("y_out", [P, BODY, 2, S])
        t_stage = sb("t_stage", [P, 2, 2, S])
        t_hi = sb("t_hi", [P, 2, 2, S], F32R)
        t_lo = sb("t_lo", [P, 2, 2, S], F32R)
        t_raw = sb("t_raw", [P, 2, 2, H])

        psz = ctx.enter_context(nc.psum_tensor("psz", [P, RING, 2, S], F32))
        psy = ctx.enter_context(nc.psum_tensor("psy", [P, RING, 2, S], F32))

        idle_ready = sem("idle_ready")
        nets_landed = sem("nets_landed")
        tables_landed = sem("tables_landed")
        mlp_product = sem("mlp_product")
        mlp_step = sem("mlp_step")
        mlp_reduced = sem("mlp_reduced")
        mlp_sine = sem("mlp_sine")
        rows_ready = sem("rows_ready")
        rows_stored = sem("rows_stored")
        x_landed = [sem(f"x_landed{q}") for q in range(PAIRS)]
        t_landed = [sem(f"t_landed{q}") for q in range(2)]
        y_stored = [sem(f"y_stored{q}") for q in range(PAIRS)]
        t_hi_done = sem("t_hi_done")
        t_raw_done = sem("t_raw_done")
        t_split = sem("t_split")
        x_hi_done = sem("x_hi_done")
        x_split = sem("x_split")
        z_product = sem("z_product")
        z_hi_done = sem("z_hi_done")
        z_lo_done = sem("z_lo_done")
        y_product = sem("y_product")
        y_done = sem("y_done")

        halves = [slice(0, ORDER), slice(ORDER, P)]
        block = ctx.enter_context(nc.Block())

        @block.sync
        def _(sp):
            def load_x(channel, slot):
                for s in (slot, slot + 1):
                    src = x[s % B, bass.ds(channel, 1), :, :].rearrange("o (k p) j -> p (o k) j", p=P)
                    sp.dma_start(x_raw[:, s, :, :], src).then_inc(x_landed[slot // 2], 16)

            def store_y(channel, slot):
                for s in (slot, slot + 1):
                    dst = out[s % B, bass.ds(channel, 1), :, :].rearrange("o (k p) j -> p (o k) j", p=P)
                    sp.dma_start(dst, y_out[:, s, :, :]).then_inc(y_stored[slot // 2], 16)

            def load_t(channel, parity):
                src = bass.AP(grev.tensor, channel * GROW, [[1, P], [C * GROW, 2], [1, S]])
                sp.dma_start(t_stage[:, parity, :, :], src).then_inc(t_landed[parity], 16)

            sp.dma_start(nets[:, :], networks).then_inc(nets_landed, 16)
            sp.dma_start(decay_sb[:, :], decay).then_inc(tables_landed, 16)
            sp.dma_start(bias_bc[:, :], bias.partition_broadcast(P)).then_inc(tables_landed, 16)
            for slot in range(0, BODY, 2):
                load_x(slot // B, slot)
            sp.wait_ge(rows_ready, 2)
            sp.dma_start(grev, grow[:, :]).then_inc(rows_stored, 16)
            sp.wait_ge(rows_stored, 16)
            load_t(0, 0)
            load_t(1, 1)
            sp.wait_ge(t_split, 1)
            sp.wait_ge(t_raw_done, 1)
            load_t(2, 0)

            def iteration(i, last):
                for m in range(1, BODY, 2):
                    sp.wait_ge(y_done, BODY * i + m + 1)
                    store_y(CHANNELS * i + m // B, m - 1)
                    if not last:
                        load_x(CHANNELS * (i + 1) + m // B, m - 1)
                    q = m // B
                    if m % B == 1 and not (last and q + 3 >= CHANNELS):
                        sp.wait_ge(t_split, CHANNELS * i + q + 2)
                        sp.wait_ge(t_raw_done, CHANNELS * i + q + 2)
                        load_t(CHANNELS * i + q + 3, (q + 3) % 2)

            with sp.Fori(0, ITERS - 1) as i:
                iteration(i, False)
            iteration(ITERS - 1, True)
            for q in range(PAIRS):
                sp.wait_ge(y_stored[q], 32 * (ITERS + 1))

        @block.tensor
        def _(pe):
            def warm_up(count):
                for _ in range(count):
                    pe.matmul(psy[:, 0, :, :], idle[:, 0:P], idle[:, :], start=True, stop=True)

            pe.wait_ge(idle_ready, 1)
            warm_up(WARM_START)
            pe.wait_ge(nets_landed, 16)
            for l in range(LAYERS + 1):
                if l:
                    pe.wait_ge(mlp_sine, l)
                for rows in halves:
                    k = slice(rows.start, rows.start + E) if l == 0 else rows
                    src = zt[k, :] if l == 0 else hidden[k, :]
                    mm = pe.matmul(psz[rows, l, 0, :], weights[l][k, :], src, start=True, stop=True)
                mm.then_inc(mlp_product, 1)
                warm_up(WARM_LAYER if l < LAYERS else WARM_WAIT)

            def product(ps, hi, lo, raw, parity, f):
                pe.matmul(ps, hi, t_hi[:, parity, f, :], start=True, stop=False)
                pe.matmul(ps, hi, t_lo[:, parity, f, :], start=False, stop=False)
                pe.matmul(ps, lo, t_hi[:, parity, f, :], start=False, stop=False)
                return pe.matmul(ps[:, 0:H], raw, t_raw[:, parity, f, :], start=False, stop=True)

            def stage1(i, m):
                s, parity = m % BODY, m // B % 2
                if m % 2 == 0:
                    pe.wait_ge(x_split, PAIRS * i + m // 2 + 1)
                if m % B == 0:
                    pe.wait_ge(t_split, CHANNELS * i + m // B + 1)
                    pe.wait_ge(t_raw_done, CHANNELS * i + m // B + 1)
                for jc in range(2):
                    j = slice(jc * P, jc * P + P)
                    mm = product(psz[:, s % RING, jc, :], x_hi[:, s % RING, j], x_lo[:, s % RING, j],
                                 x_raw[:, s, 1, j], parity, 0)
                mm.then_inc(z_product, 1)

            def stage2(i, m):
                s, parity = m % RING, m // B % 2
                pe.wait_ge(z_lo_done, BODY * i + m + 1)
                for ic in range(2):
                    r = slice(ic * P, ic * P + P)
                    mm = product(psy[:, s, ic, :], z_hi[:, s, r], z_lo[:, s, r], z_raw[:, s, r], parity, 1)
                mm.then_inc(y_product, 1)

            for m in range(LEAD):
                stage1(0, m)

            def iteration(i, last):
                for m in range(BODY):
                    if not last or m + LEAD < BODY:
                        stage1(i, m + LEAD)
                    stage2(i, m)

            with pe.Fori(0, ITERS - 1) as i:
                iteration(i, False)
            iteration(ITERS - 1, True)

        @block.scalar
        def _(act):
            for l in range(LAYERS):
                act.wait_ge(mlp_reduced, l + 1)
                nc.scalar.activation(hidden[:, :], red[:, 2, :], ACT.Sin).then_inc(mlp_sine, 1)

            def split_t(channel, parity, landed):
                act.wait_ge(t_landed[parity], landed)
                nc.scalar.copy(t_hi[:, parity, :, :], t_stage[:, parity, :, :]).then_inc(t_hi_done, 1)
                nc.scalar.copy(t_raw[:, parity, :, :], t_stage[:, parity, :, H:S]).then_inc(t_raw_done, 1)

            def split_x(slot, landed):
                act.wait_ge(x_landed[slot // 2], landed)
                r = slot % RING
                nc.scalar.copy(x_hi[:, r:r + 2, :], x_raw[:, slot:slot + 2, 0, :]).then_inc(x_hi_done, 1)

            def evacuate(i, m):
                s = m % RING
                act.wait_ge(z_product, BODY * i + m + 1)
                nc.scalar.copy(z_raw[:, s, :], backwards(psz[:, s, 1, :]))
                nc.scalar.copy(z_hi[:, s, :], backwards(psz[:, s, 0, :])).then_inc(z_hi_done, 1)

            split_x(0, 32)
            split_x(2, 32)
            split_t(0, 0, 16)
            for m in range(LEAD):
                evacuate(0, m)

            def iteration(i, last):
                for m in range(BODY):
                    if not last or m + LEAD < BODY:
                        evacuate(i, m + LEAD)
                    if m % 2 == 0 and not (last and m + RING >= BODY):
                        split_x((m + RING) % BODY, 32 * (i + 1 + (m + RING) // BODY))
                    q = m // B + 1
                    if m % B == 0 and not (last and q >= CHANNELS):
                        split_t(CHANNELS * i + q, q % 2, 16 * (CHANNELS // 2 * i + q // 2 + 1))

            with act.Fori(0, ITERS - 1) as i:
                iteration(i, False)
            iteration(ITERS - 1, True)

        @block.vector
        def _(dve):
            steps = [0]

            def step(ins):
                steps[0] += 1
                ins.then_inc(mlp_step, 1)
                dve.wait_ge(mlp_step, steps[0])

            nc.vector.memset(idle[:, :], 0.0).then_inc(idle_ready, 1)
            for q in range(PAIRS):
                dve.sem_inc(y_stored[q], 32)
            nc.vector.memset(grow[:, S:GROW], 0.0).then_inc(rows_ready, 1)
            dve.wait_ge(nets_landed, 16)
            for l in range(LAYERS):
                dve.wait_ge(mlp_product, l + 1)
                step(nc.vector.tensor_scalar(angle[:, :], psz[:, l, 0, :], cols[:, l:l + 1],
                                             cols[:, LAYERS:LAYERS + 1], ALU.add, ALU.mult))
                step(nc.vector.tensor_scalar(turns[:, :], angle[:, :], 1.0 / TWO_PI, ROUND, ALU.mult, ALU.add))
                step(nc.vector.tensor_scalar(whole[:, :], turns[:, :], ROUND, None, ALU.subtract))
                step(nc.vector.scalar_tensor_tensor(out=red[:, 0, :], in0=whole[:, :], scalar=-PI_A,
                                                    in1=angle[:, :], op0=ALU.mult, op1=ALU.add))
                step(nc.vector.scalar_tensor_tensor(out=red[:, 1, :], in0=whole[:, :], scalar=-PI_B,
                                                    in1=red[:, 0, :], op0=ALU.mult, op1=ALU.add))
                nc.vector.tensor_scalar(red[:, 2, :], red[:, 1, :], PI_INSIDE, -PI_INSIDE,
                                        ALU.min, ALU.max).then_inc(mlp_reduced, 1)
            dve.wait_ge(tables_landed, 32)
            dve.wait_ge(mlp_product, LAYERS + 1)
            nc.vector.tensor_tensor(backwards(grow[:, 0:S]), psz[:, LAYERS, 0, :], decay_sb[:, :],
                                    ALU.mult).then_inc(rows_ready, 1)

            def split_t(channel, parity):
                dve.wait_ge(t_hi_done, channel + 1)
                nc.vector.tensor_tensor(t_lo[:, parity, :, :], t_stage[:, parity, :, :],
                                        t_hi[:, parity, :, :].bitcast(F32), ALU.subtract).then_inc(t_split, 1)

            def split_x(pair, slot):
                dve.wait_ge(x_hi_done, pair + 1)
                r = slot % RING
                nc.vector.tensor_tensor(x_lo[:, r:r + 2, :], x_raw[:, slot:slot + 2, 0, :],
                                        x_hi[:, r:r + 2, :].bitcast(F32), ALU.subtract).then_inc(x_split, 1)

            def split_z(i, m):
                s = m % RING
                dve.wait_ge(z_hi_done, BODY * i + m + 1)
                nc.vector.tensor_tensor(z_lo[:, s, :], backwards(psz[:, s, 0, :]), z_hi[:, s, :].bitcast(F32),
                                        ALU.subtract).then_inc(z_lo_done, 1)

            def finish_y(i, m):
                dve.wait_ge(y_product, BODY * i + m + 1)
                if m % 2 == 0:
                    dve.wait_ge(y_stored[m // 2], 32 * (i + 1))
                nc.vector.scalar_tensor_tensor(out=y_out[:, m, :, :], in0=x_raw[:, m, :, :],
                                               scalar=bias_bc[:, bass.ds(CHANNELS * i + m // B, 1)],
                                               in1=backwards(psy[:, m % RING, :, :]),
                                               op0=ALU.mult, op1=ALU.add).then_inc(y_done, 1)

            split_x(0, 0)
            split_x(1, 2)
            split_t(0, 0)
            for m in range(LEAD):
                split_z(0, m)

            def iteration(i, last):
                for m in range(BODY):
                    if not last or m + LEAD < BODY:
                        split_z(i, m + LEAD)
                    if m % 2 == 0 and not (last and m + RING >= BODY):
                        split_x(PAIRS * i + (m + RING) // 2, (m + RING) % BODY)
                    q = m // B + 1
                    if m % B == 0 and not (last and q >= CHANNELS):
                        split_t(CHANNELS * i + q, q % 2)
                    finish_y(i, m)

            with dve.Fori(0, ITERS - 1) as i:
                iteration(i, False)
            iteration(ITERS - 1, True)


def kernel(**inputs):
    import concourse.bacc as _bacc
    from concourse.bass_utils import run_bass_kernel_spmd as _run

    nc = _bacc.Bacc("TRN2", target_bir_lowering=False, num_devices=1)
    arrays = {}

    def given(name, a):
        a = np.ascontiguousarray(a)
        arrays[name] = a
        return nc.dram_tensor(name, a.shape, mybir.dt.from_np(a.dtype), kind="ExternalInput").ap()

    x = np.asarray(inputs["x"])
    _, channels, seq, _ = x.shape

    z_t = np.asarray(inputs["L0_conv_z"])[0].T
    embedding, order = z_t.shape[0], inputs["L0_conv_Xw2"].shape[0]
    networks = np.zeros((2 * order, seq + (LAYERS + 1) * order + LAYERS + 1), np.float32)
    for f, rows in (("X", 0), ("Y", order)):
        networks[rows:rows + embedding, 0:seq] = z_t
        at = seq
        for name in ("w1", "w2", "w3", "wo", "b1", "b2", "b3", "freq"):
            a = np.asarray(inputs[f"L0_conv_{f}{name}"])
            a = a if name[0] == "w" else a.reshape(-1, 1)
            networks[rows:rows + a.shape[0], at:at + a.shape[1]] = a
            at += a.shape[1]

    args = [
        given("x_dram", x),
        given("networks", networks),
        given("bias_dram", inputs["L0_conv_bias"]),
        given("decay", decay_table(seq, channels, 2 * seq)),
    ]
    out = nc.dram_tensor("out_dram", x.shape, mybir.dt.from_np(x.dtype), kind="ExternalOutput").ap()
    build_program(nc, *args, out, embedding, order)
    r = _run(nc, [arrays], core_ids=[0])
    return r.results[0]["out_dram"]
```

```python
import math
from contextlib import ExitStack

import numpy as np

import concourse.bass as bass
from concourse import mybir

F32 = mybir.dt.float32
F32R = mybir.dt.float32r
ALU = mybir.AluOpType
ACT = mybir.ActivationFunctionType

P = 128
H = P
TWO_PI = 2.0 * math.pi
PI_A = 6.28125
PI_B = TWO_PI - PI_A
ROUND = 1.5 * 2.0 ** 23
PI_INSIDE = 3.1415925

LAYERS = 3
STEPS = 5
RING = 4
BODY = 16
LEAD = 2
WARM_START = 5
WARM_LAYER = (6, 8, 8, 30)


def decay_table(seq, channels, fft_size):
    t = np.linspace(0.0, 1.0, seq).astype(np.float32)
    deltas = np.linspace(math.log(0.01) / 1.5, math.log(0.01) / 0.3, channels).astype(np.float32)
    decay = np.exp(-(t[None, :] * np.abs(deltas)[:, None])).astype(np.float32)
    return np.concatenate([decay, decay / np.float32(fft_size)], axis=0)


def backwards(ap):
    step, count = ap.ap[-1]
    return bass.AP(ap.tensor, ap.offset + step * (count - 1), [*ap.ap[:-1], [-step, count]])


def build_program(nc, x, networks, bias, decay, out, E, ORDER):
    B, C, S, _ = x.shape
    N = B * C
    assert S == 2 * H and 2 * C == P and 2 * ORDER == P
    assert B == RING and BODY % (2 * B) == 0 and BODY > 2 * B and N % BODY == 0
    ITERS = N // BODY
    CHANNELS = BODY // B
    PAIRS = BODY // 2
    GROW = S + P

    grev = nc.dram_tensor("filters_reversed", (P, GROW), F32, kind="Internal").ap()

    with ExitStack() as ctx:
        def sb(name, shape, dt=F32):
            return ctx.enter_context(nc.sbuf_tensor(name, shape, dt))

        def sem(name):
            return ctx.enter_context(nc.semaphore(name))

        nets = sb("nets", [P, networks.shape[1]])
        zt = nets[:, 0:S]
        weights = [nets[:, S + l * ORDER:S + (l + 1) * ORDER] for l in range(LAYERS + 1)]
        cols = nets[:, S + (LAYERS + 1) * ORDER:]
        decay_sb = sb("decay_sb", [P, S])
        bias_bc = sb("bias_bc", [P, C])
        angle = sb("angle", [P, S])
        turns = sb("turns", [P, S])
        whole = sb("whole", [P, S])
        partly = sb("partly", [P, S])
        nearly = sb("nearly", [P, S])
        reduced = sb("reduced", [P, S])
        hidden = sb("hidden", [P, S])
        grow = sb("grow", [P, GROW])
        idle = sb("idle", [P, 2 * S], mybir.dt.bfloat16)

        x_raw = sb("x_raw", [P, BODY, 2, S])
        x_hi = sb("x_hi", [P, RING, S], F32R)
        x_lo = sb("x_lo", [P, RING, S], F32R)
        z_hi = sb("z_hi", [P, RING, S], F32R)
        z_lo = sb("z_lo", [P, RING, S], F32R)
        z_raw = sb("z_raw", [P, RING, S])
        y_out = sb("y_out", [P, BODY, 2, S])
        t_stage = sb("t_stage", [P, 2, 2, S])
        t_hi = sb("t_hi", [P, 2, 2, S], F32R)
        t_lo = sb("t_lo", [P, 2, 2, S], F32R)
        t_raw = sb("t_raw", [P, 2, 2, H])

        psz = ctx.enter_context(nc.psum_tensor("psz", [P, RING, 2, S], F32))
        psy = ctx.enter_context(nc.psum_tensor("psy", [P, RING, 2, S], F32))

        idle_ready = sem("idle_ready")
        nets_landed = sem("nets_landed")
        tables_landed = sem("tables_landed")
        mlp_product = sem("mlp_product")
        mlp_step = sem("mlp_step")
        mlp_reduced = sem("mlp_reduced")
        mlp_sine = sem("mlp_sine")
        rows_ready = sem("rows_ready")
        rows_stored = sem("rows_stored")
        x_landed = [sem(f"x_landed{q}") for q in range(PAIRS)]
        t_landed = [sem(f"t_landed{q}") for q in range(2)]
        y_stored = [sem(f"y_stored{q}") for q in range(PAIRS)]
        first_hi = sem("first_hi")
        first_split = sem("first_split")
        t_hi_done = sem("t_hi_done")
        t_raw_done = sem("t_raw_done")
        t_split = sem("t_split")
        x_hi_done = sem("x_hi_done")
        x_split = sem("x_split")
        z_product = sem("z_product")
        z_hi_done = sem("z_hi_done")
        z_lo_done = sem("z_lo_done")
        y_product = sem("y_product")
        y_done = sem("y_done")

        halves = [slice(0, ORDER), slice(ORDER, P)]
        spans = [slice(0, H), slice(H, S)]

        def layer_product(l, h):
            return psz[:, 2 * (l % 2) + h, 0, 0:H]

        block = ctx.enter_context(nc.Block())

        @block.sync
        def _(sp):
            def load_x(channel, slot):
                for s in (slot, slot + 1):
                    src = x[s % B, bass.ds(channel, 1), :, :].rearrange("o (k p) j -> p (o k) j", p=P)
                    sp.dma_start(x_raw[:, s, :, :], src).then_inc(x_landed[slot // 2], 16)

            def store_y(channel, slot):
                for s in (slot, slot + 1):
                    dst = out[s % B, bass.ds(channel, 1), :, :].rearrange("o (k p) j -> p (o k) j", p=P)
                    sp.dma_start(dst, y_out[:, s, :, :]).then_inc(y_stored[slot // 2], 16)

            def load_t(channel, parity):
                src = bass.AP(grev.tensor, channel * GROW, [[1, P], [C * GROW, 2], [1, S]])
                sp.dma_start(t_stage[:, parity, :, :], src).then_inc(t_landed[parity], 16)

            sp.dma_start(nets[:, :], networks).then_inc(nets_landed, 16)
            sp.dma_start(decay_sb[:, :], decay).then_inc(tables_landed, 16)
            sp.dma_start(bias_bc[:, :], bias.partition_broadcast(P)).then_inc(tables_landed, 16)
            for slot in range(0, BODY, 2):
                load_x(slot // B, slot)
            sp.wait_ge(rows_ready, 3)
            sp.dma_start(grev, grow[:, :]).then_inc(rows_stored, 16)
            sp.wait_ge(rows_stored, 16)
            load_t(0, 0)
            load_t(1, 1)
            sp.wait_ge(t_split, 1)
            sp.wait_ge(t_raw_done, 1)
            load_t(2, 0)

            def iteration(i, last):
                for m in range(1, BODY, 2):
                    sp.wait_ge(y_done, BODY * i + m + 1)
                    store_y(CHANNELS * i + m // B, m - 1)
                    if not last:
                        load_x(CHANNELS * (i + 1) + m // B, m - 1)
                    q = m // B
                    if m % B == 1 and not (last and q + 3 >= CHANNELS):
                        sp.wait_ge(t_split, CHANNELS * i + q + 2)
                        sp.wait_ge(t_raw_done, CHANNELS * i + q + 2)
                        load_t(CHANNELS * i + q + 3, (q + 3) % 2)

            with sp.Fori(0, ITERS - 1) as i:
                iteration(i, False)
            iteration(ITERS - 1, True)
            for q in range(PAIRS):
                sp.wait_ge(y_stored[q], 32 * (ITERS + 1))

        @block.tensor
        def _(pe):
            def warm_up(count):
                for _ in range(count):
                    pe.matmul(psy[:, 0, :, :], idle[:, 0:P], idle[:, :], start=True, stop=True)

            pe.wait_ge(idle_ready, 1)
            warm_up(WARM_START)
            pe.wait_ge(nets_landed, 16)
            for l in range(LAYERS + 1):
                for h, t in enumerate(spans):
                    if l:
                        pe.wait_ge(mlp_sine, 2 * (l - 1) + h + 1)
                    for rows in halves:
                        k = slice(rows.start, rows.start + E) if l == 0 else rows
                        src = zt[k, t] if l == 0 else hidden[k, t]
                        mm = pe.matmul(layer_product(l, h)[rows, :], weights[l][k, :], src,
                                       start=True, stop=True)
                    mm.then_inc(mlp_product, 1)
                warm_up(WARM_LAYER[l])

            def product(ps, hi, lo, raw, parity, f):
                pe.matmul(ps, hi, t_hi[:, parity, f, :], start=True, stop=False)
                pe.matmul(ps, hi, t_lo[:, parity, f, :], start=False, stop=False)
                pe.matmul(ps, lo, t_hi[:, parity, f, :], start=False, stop=False)
                return pe.matmul(ps[:, 0:H], raw, t_raw[:, parity, f, :], start=False, stop=True)

            def stage1(i, m, first=False):
                s, parity = m % BODY, m // B % 2
                if m % 2 == 0:
                    pe.wait_ge(x_split, PAIRS * i + m // 2 + 1)
                if m % B == 0 and not first:
                    pe.wait_ge(t_split, CHANNELS * i + m // B + 1)
                    pe.wait_ge(t_raw_done, CHANNELS * i + m // B + 1)
                elif m == 0:
                    pe.wait_ge(first_split, 1)
                for jc in range(2):
                    j = slice(jc * P, jc * P + P)
                    mm = product(psz[:, s % RING, jc, :], x_hi[:, s % RING, j], x_lo[:, s % RING, j],
                                 x_raw[:, s, 1, j], parity, 0)
                mm.then_inc(z_product, 1)

            def stage2(i, m):
                s, parity = m % RING, m // B % 2
                pe.wait_ge(z_lo_done, BODY * i + m + 1)
                for ic in range(2):
                    r = slice(ic * P, ic * P + P)
                    mm = product(psy[:, s, ic, :], z_hi[:, s, r], z_lo[:, s, r], z_raw[:, s, r], parity, 1)
                mm.then_inc(y_product, 1)

            for m in range(LEAD):
                stage1(0, m, first=True)
            pe.wait_ge(t_split, 1)
            pe.wait_ge(t_raw_done, 1)

            def iteration(i, last):
                for m in range(BODY):
                    if not last or m + LEAD < BODY:
                        stage1(i, m + LEAD)
                    stage2(i, m)

            with pe.Fori(0, ITERS - 1) as i:
                iteration(i, False)
            iteration(ITERS - 1, True)

        @block.scalar
        def _(act):
            for l in range(LAYERS):
                for h, t in enumerate(spans):
                    act.wait_ge(mlp_reduced, 2 * l + h + 1)
                    nc.scalar.activation(hidden[:, t], reduced[:, t], ACT.Sin).then_inc(mlp_sine, 1)

            def split_t(channel, parity, landed):
                act.wait_ge(t_landed[parity], landed)
                nc.scalar.copy(t_hi[:, parity, :, :], t_stage[:, parity, :, :]).then_inc(t_hi_done, 1)
                nc.scalar.copy(t_raw[:, parity, :, :], t_stage[:, parity, :, H:S]).then_inc(t_raw_done, 1)

            def split_x(slot, landed):
                act.wait_ge(x_landed[slot // 2], landed)
                r = slot % RING
                nc.scalar.copy(x_hi[:, r:r + 2, :], x_raw[:, slot:slot + 2, 0, :]).then_inc(x_hi_done, 1)

            def evacuate(i, m):
                s = m % RING
                act.wait_ge(z_product, BODY * i + m + 1)
                nc.scalar.copy(z_raw[:, s, :], backwards(psz[:, s, 1, :]))
                nc.scalar.copy(z_hi[:, s, :], backwards(psz[:, s, 0, :])).then_inc(z_hi_done, 1)

            split_x(0, 32)
            split_x(2, 32)
            act.wait_ge(t_landed[0], 16)
            nc.scalar.copy(t_hi[:, 0, 0, :], t_stage[:, 0, 0, :]).then_inc(first_hi, 1)
            nc.scalar.copy(t_raw[:, 0, 0, :], t_stage[:, 0, 0, H:S]).then_inc(first_hi, 1)
            nc.scalar.copy(t_hi[:, 0, 1, :], t_stage[:, 0, 1, :]).then_inc(t_hi_done, 1)
            nc.scalar.copy(t_raw[:, 0, 1, :], t_stage[:, 0, 1, H:S]).then_inc(t_raw_done, 1)
            for m in range(LEAD):
                evacuate(0, m)

            def iteration(i, last):
                for m in range(BODY):
                    if not last or m + LEAD < BODY:
                        evacuate(i, m + LEAD)
                    if m % 2 == 0 and not (last and m + RING >= BODY):
                        split_x((m + RING) % BODY, 32 * (i + 1 + (m + RING) // BODY))
                    q = m // B + 1
                    if m % B == 0 and not (last and q >= CHANNELS):
                        split_t(CHANNELS * i + q, q % 2, 16 * (CHANNELS // 2 * i + q // 2 + 1))

            with act.Fori(0, ITERS - 1) as i:
                iteration(i, False)
            iteration(ITERS - 1, True)

        @block.vector
        def _(dve):
            nc.vector.memset(idle[:, :], 0.0).then_inc(idle_ready, 1)
            for q in range(PAIRS):
                dve.sem_inc(y_stored[q], 32)
            nc.vector.memset(grow[:, S:GROW], 0.0).then_inc(rows_ready, 1)
            dve.wait_ge(nets_landed, 16)

            def after(l, number, h):
                return STEPS * 2 * l + 2 * number + h + 1

            for l in range(LAYERS):
                for h, t in enumerate(spans):
                    dve.wait_ge(mlp_product, 2 * l + h + 1)
                    nc.vector.tensor_scalar(angle[:, t], layer_product(l, h), cols[:, l:l + 1],
                                            cols[:, LAYERS:LAYERS + 1], ALU.add, ALU.mult).then_inc(mlp_step, 1)
                for h, t in enumerate(spans):
                    dve.wait_ge(mlp_step, after(l, 0, h))
                    nc.vector.tensor_scalar(turns[:, t], angle[:, t], 1.0 / TWO_PI, ROUND,
                                            ALU.mult, ALU.add).then_inc(mlp_step, 1)
                for h, t in enumerate(spans):
                    dve.wait_ge(mlp_step, after(l, 1, h))
                    nc.vector.tensor_scalar(whole[:, t], turns[:, t], ROUND, None,
                                            ALU.subtract).then_inc(mlp_step, 1)
                for h, t in enumerate(spans):
                    dve.wait_ge(mlp_step, after(l, 2, h))
                    nc.vector.scalar_tensor_tensor(out=partly[:, t], in0=whole[:, t], scalar=-PI_A,
                                                   in1=angle[:, t], op0=ALU.mult,
                                                   op1=ALU.add).then_inc(mlp_step, 1)
                for h, t in enumerate(spans):
                    dve.wait_ge(mlp_step, after(l, 3, h))
                    nc.vector.scalar_tensor_tensor(out=nearly[:, t], in0=whole[:, t], scalar=-PI_B,
                                                   in1=partly[:, t], op0=ALU.mult,
                                                   op1=ALU.add).then_inc(mlp_step, 1)
                for h, t in enumerate(spans):
                    dve.wait_ge(mlp_step, after(l, 4, h))
                    nc.vector.tensor_scalar(reduced[:, t], nearly[:, t], PI_INSIDE, -PI_INSIDE,
                                            ALU.min, ALU.max).then_inc(mlp_reduced, 1)
            dve.wait_ge(tables_landed, 32)
            for h, t in enumerate(spans):
                dve.wait_ge(mlp_product, 2 * LAYERS + h + 1)
                nc.vector.tensor_tensor(backwards(grow[:, S - t.stop:S - t.start]), layer_product(LAYERS, h),
                                        decay_sb[:, t], ALU.mult).then_inc(rows_ready, 1)

            def split_t(channel, parity):
                dve.wait_ge(t_hi_done, channel + 1)
                nc.vector.tensor_tensor(t_lo[:, parity, :, :], t_stage[:, parity, :, :],
                                        t_hi[:, parity, :, :].bitcast(F32), ALU.subtract).then_inc(t_split, 1)

            def split_x(pair, slot):
                dve.wait_ge(x_hi_done, pair + 1)
                r = slot % RING
                nc.vector.tensor_tensor(x_lo[:, r:r + 2, :], x_raw[:, slot:slot + 2, 0, :],
                                        x_hi[:, r:r + 2, :].bitcast(F32), ALU.subtract).then_inc(x_split, 1)

            def split_z(i, m):
                s = m % RING
                dve.wait_ge(z_hi_done, BODY * i + m + 1)
                nc.vector.tensor_tensor(z_lo[:, s, :], backwards(psz[:, s, 0, :]), z_hi[:, s, :].bitcast(F32),
                                        ALU.subtract).then_inc(z_lo_done, 1)

            def finish_y(i, m):
                dve.wait_ge(y_product, BODY * i + m + 1)
                if m % 2 == 0:
                    dve.wait_ge(y_stored[m // 2], 32 * (i + 1))
                nc.vector.scalar_tensor_tensor(out=y_out[:, m, :, :], in0=x_raw[:, m, :, :],
                                               scalar=bias_bc[:, bass.ds(CHANNELS * i + m // B, 1)],
                                               in1=backwards(psy[:, m % RING, :, :]),
                                               op0=ALU.mult, op1=ALU.add).then_inc(y_done, 1)

            split_x(0, 0)
            split_x(1, 2)
            dve.wait_ge(first_hi, 2)
            nc.vector.tensor_tensor(t_lo[:, 0, 0, :], t_stage[:, 0, 0, :], t_hi[:, 0, 0, :].bitcast(F32),
                                    ALU.subtract).then_inc(first_split, 1)
            dve.wait_ge(t_hi_done, 1)
            nc.vector.tensor_tensor(t_lo[:, 0, 1, :], t_stage[:, 0, 1, :], t_hi[:, 0, 1, :].bitcast(F32),
                                    ALU.subtract).then_inc(t_split, 1)
            for m in range(LEAD):
                split_z(0, m)

            def iteration(i, last):
                for m in range(BODY):
                    if not last or m + LEAD < BODY:
                        split_z(i, m + LEAD)
                    if m % 2 == 0 and not (last and m + RING >= BODY):
                        split_x(PAIRS * i + (m + RING) // 2, (m + RING) % BODY)
                    q = m // B + 1
                    if m % B == 0 and not (last and q >= CHANNELS):
                        split_t(CHANNELS * i + q, q % 2)
                    finish_y(i, m)

            with dve.Fori(0, ITERS - 1) as i:
                iteration(i, False)
            iteration(ITERS - 1, True)


def kernel(**inputs):
    import concourse.bacc as _bacc
    from concourse.bass_utils import run_bass_kernel_spmd as _run

    nc = _bacc.Bacc("TRN2", target_bir_lowering=False, num_devices=1)
    arrays = {}

    def given(name, a):
        a = np.ascontiguousarray(a)
        arrays[name] = a
        return nc.dram_tensor(name, a.shape, mybir.dt.from_np(a.dtype), kind="ExternalInput").ap()

    x = np.asarray(inputs["x"])
    _, channels, seq, _ = x.shape

    z_t = np.asarray(inputs["L0_conv_z"])[0].T
    embedding, order = z_t.shape[0], inputs["L0_conv_Xw2"].shape[0]
    networks = np.zeros((2 * order, seq + (LAYERS + 1) * order + LAYERS + 1), np.float32)
    for f, rows in (("X", 0), ("Y", order)):
        networks[rows:rows + embedding, 0:seq] = z_t
        at = seq
        for name in ("w1", "w2", "w3", "wo", "b1", "b2", "b3", "freq"):
            a = np.asarray(inputs[f"L0_conv_{f}{name}"])
            a = a if name[0] == "w" else a.reshape(-1, 1)
            networks[rows:rows + a.shape[0], at:at + a.shape[1]] = a
            at += a.shape[1]

    args = [
        given("x_dram", x),
        given("networks", networks),
        given("bias_dram", inputs["L0_conv_bias"]),
        given("decay", decay_table(seq, channels, 2 * seq)),
    ]
    out = nc.dram_tensor("out_dram", x.shape, mybir.dt.from_np(x.dtype), kind="ExternalOutput").ap()
    build_program(nc, *args, out, embedding, order)
    r = _run(nc, [arrays], core_ids=[0])
    return r.results[0]["out_dram"]
```
